# Optimizing a Trainium2 kernel written in Bass

```python
import numpy as np
import jax
import jax.numpy as jnp

def _softmax(x, axis=-1):
    return jax.nn.softmax(x, axis=axis)

def _gelu(x):
    return jax.nn.gelu(x, approximate=True)

def _silu(x):
    return jax.nn.silu(x)

def _sigmoid(x):
    return jax.nn.sigmoid(x)

def _layernorm(x, axis=-1, eps=1e-05):
    m = jnp.mean(x, axis=axis, keepdims=True)
    v = jnp.var(x, axis=axis, keepdims=True)
    return (x - m) / jnp.sqrt(v + eps)

def _scatter_add(tgt, idx, src, axis=0):
    return tgt.at[idx].add(src)

def _segment_sum(src, seg, n):
    return jax.ops.segment_sum(src, seg, n)
kernel_name = 'mk_dlrm_tower_d1_rec_r8_578936'

def setup_inputs(seed: int=0):
    np.random.seed(seed)
    _w = jnp.asarray

    def _rec_inputs():
        import jax
        import jax.numpy as jnp
        _tk = jax.random.key(seed)
        dense_ctx = jax.random.normal(jax.random.fold_in(_tk, 190), (1024, 16), jnp.float32)
        ids = jnp.stack([jax.random.randint(jax.random.fold_in(_tk, 200 + f), (1024,), 0, v, jnp.int32) for f, v in enumerate([1250, 125000, 12500, 12500, 1250, 1000, 1000, 125000, 1000, 125000, 12500, 1250, 1250, 1250, 1000, 12500, 1000, 1250, 1250, 1250, 1000, 1250, 1000, 1000, 12500, 1000, 1250, 12500, 1000, 1250, 1000, 1000])], axis=1)
        tbl_0 = 0.05 * jax.random.normal(jax.random.fold_in(_tk, 500 + 0), (1250, 64), jnp.float32)
        tbl_1 = 0.05 * jax.random.normal(jax.random.fold_in(_tk, 500 + 1), (125000, 64), jnp.float32)
        tbl_2 = 0.05 * jax.random.normal(jax.random.fold_in(_tk, 500 + 2), (12500, 64), jnp.float32)
        tbl_3 = 0.05 * jax.random.normal(jax.random.fold_in(_tk, 500 + 3), (12500, 64), jnp.float32)
        tbl_4 = 0.05 * jax.random.normal(jax.random.fold_in(_tk, 500 + 4), (1250, 64), jnp.float32)
        tbl_5 = 0.05 * jax.random.normal(jax.random.fold_in(_tk, 500 + 5), (1000, 64), jnp.float32)
        tbl_6 = 0.05 * jax.random.normal(jax.random.fold_in(_tk, 500 + 6), (1000, 64), jnp.float32)
        tbl_7 = 0.05 * jax.random.normal(jax.random.fold_in(_tk, 500 + 7), (125000, 64), jnp.float32)
        tbl_8 = 0.05 * jax.random.normal(jax.random.fold_in(_tk, 500 + 8), (1000, 64), jnp.float32)
        tbl_9 = 0.05 * jax.random.normal(jax.random.fold_in(_tk, 500 + 9), (125000, 64), jnp.float32)
        tbl_10 = 0.05 * jax.random.normal(jax.random.fold_in(_tk, 500 + 10), (12500, 64), jnp.float32)
        tbl_11 = 0.05 * jax.random.normal(jax.random.fold_in(_tk, 500 + 11), (1250, 64), jnp.float32)
        tbl_12 = 0.05 * jax.random.normal(jax.random.fold_in(_tk, 500 + 12), (1250, 64), jnp.float32)
        tbl_13 = 0.05 * jax.random.normal(jax.random.fold_in(_tk, 500 + 13), (1250, 64), jnp.float32)
        tbl_14 = 0.05 * jax.random.normal(jax.random.fold_in(_tk, 500 + 14), (1000, 64), jnp.float32)
        tbl_15 = 0.05 * jax.random.normal(jax.random.fold_in(_tk, 500 + 15), (12500, 64), jnp.float32)
        tbl_16 = 0.05 * jax.random.normal(jax.random.fold_in(_tk, 500 + 16), (1000, 64), jnp.float32)
        tbl_17 = 0.05 * jax.random.normal(jax.random.fold_in(_tk, 500 + 17), (1250, 64), jnp.float32)
        tbl_18 = 0.05 * jax.random.normal(jax.random.fold_in(_tk, 500 + 18), (1250, 64), jnp.float32)
        tbl_19 = 0.05 * jax.random.normal(jax.random.fold_in(_tk, 500 + 19), (1250, 64), jnp.float32)
        tbl_20 = 0.05 * jax.random.normal(jax.random.fold_in(_tk, 500 + 20), (1000, 64), jnp.float32)
        tbl_21 = 0.05 * jax.random.normal(jax.random.fold_in(_tk, 500 + 21), (1250, 64), jnp.float32)
        tbl_22 = 0.05 * jax.random.normal(jax.random.fold_in(_tk, 500 + 22), (1000, 64), jnp.float32)
        tbl_23 = 0.05 * jax.random.normal(jax.random.fold_in(_tk, 500 + 23), (1000, 64), jnp.float32)
        tbl_24 = 0.05 * jax.random.normal(jax.random.fold_in(_tk, 500 + 24), (12500, 64), jnp.float32)
        tbl_25 = 0.05 * jax.random.normal(jax.random.fold_in(_tk, 500 + 25), (1000, 64), jnp.float32)
        tbl_26 = 0.05 * jax.random.normal(jax.random.fold_in(_tk, 500 + 26), (1250, 64), jnp.float32)
        tbl_27 = 0.05 * jax.random.normal(jax.random.fold_in(_tk, 500 + 27), (12500, 64), jnp.float32)
        tbl_28 = 0.05 * jax.random.normal(jax.random.fold_in(_tk, 500 + 28), (1000, 64), jnp.float32)
        tbl_29 = 0.05 * jax.random.normal(jax.random.fold_in(_tk, 500 + 29), (1250, 64), jnp.float32)
        tbl_30 = 0.05 * jax.random.normal(jax.random.fold_in(_tk, 500 + 30), (1000, 64), jnp.float32)
        tbl_31 = 0.05 * jax.random.normal(jax.random.fold_in(_tk, 500 + 31), (1000, 64), jnp.float32)
        _rk = jax.random.fold_in(_tk, 7)
        W_top1 = 0.0606339 * jax.random.normal(jax.random.fold_in(_tk, 801), (272, 512), jnp.float32)
        W_top2 = 0.0441942 * jax.random.normal(jax.random.fold_in(_tk, 802), (512, 256), jnp.float32)
        W_top3 = 0.0625 * jax.random.normal(jax.random.fold_in(_tk, 803), (256, 1), jnp.float32)
        b_top1 = jnp.zeros((512,), jnp.float32)
        b_top2 = jnp.zeros((256,), jnp.float32)
        return (dense_ctx, ids, tbl_0, tbl_1, tbl_2, tbl_3, tbl_4, tbl_5, tbl_6, tbl_7, tbl_8, tbl_9, tbl_10, tbl_11, tbl_12, tbl_13, tbl_14, tbl_15, tbl_16, tbl_17, tbl_18, tbl_19, tbl_20, tbl_21, tbl_22, tbl_23, tbl_24, tbl_25, tbl_26, tbl_27, tbl_28, tbl_29, tbl_30, tbl_31, W_top1, b_top1, W_top2, b_top2, W_top3)
    dense_ctx, ids, tbl_0, tbl_1, tbl_2, tbl_3, tbl_4, tbl_5, tbl_6, tbl_7, tbl_8, tbl_9, tbl_10, tbl_11, tbl_12, tbl_13, tbl_14, tbl_15, tbl_16, tbl_17, tbl_18, tbl_19, tbl_20, tbl_21, tbl_22, tbl_23, tbl_24, tbl_25, tbl_26, tbl_27, tbl_28, tbl_29, tbl_30, tbl_31, W_top1, b_top1, W_top2, b_top2, W_top3 = _rec_inputs()

    def _L0_rec_setup():
        import jax, jax.numpy as jnp
        import numpy as np
        EMB_DIM = 64
        NUM_FIELDS = 32
        NUM_PAIRS = NUM_FIELDS * (NUM_FIELDS - 1) // 2
        D1 = 256
        BATCH = 256
        key = jax.random.key(seed)
        k1, k2, k3 = jax.random.split(key, 3)
        feat_emb = jax.random.normal(k1, (BATCH, NUM_FIELDS, EMB_DIM), dtype=jnp.float32)
        lim_k = float(np.sqrt(6.0 / (EMB_DIM + EMB_DIM)))
        kernel = jax.random.uniform(k2, (EMB_DIM, NUM_PAIRS, EMB_DIM), minval=-lim_k, maxval=lim_k, dtype=jnp.float32)
        lim_w = float(np.sqrt(6.0 / (NUM_PAIRS + D1)))
        W = jax.random.uniform(k3, (D1, NUM_PAIRS), minval=-lim_w, maxval=lim_w, dtype=jnp.float32)
        b = jnp.zeros((D1,), dtype=jnp.float32)
        return {'feat_emb': feat_emb, 'kernel': kernel, 'W': W, 'b': b}
    _L0_rec_all = _L0_rec_setup()
    _L0_rec_in = {k: v for k, v in _L0_rec_all.items() if k in ('kernel', 'W', 'b')}
    del _L0_rec_all
    return {'dense_ctx': dense_ctx, 'ids': ids, 'tbl_0': tbl_0, 'tbl_1': tbl_1, 'tbl_2': tbl_2, 'tbl_3': tbl_3, 'tbl_4': tbl_4, 'tbl_5': tbl_5, 'tbl_6': tbl_6, 'tbl_7': tbl_7, 'tbl_8': tbl_8, 'tbl_9': tbl_9, 'tbl_10': tbl_10, 'tbl_11': tbl_11, 'tbl_12': tbl_12, 'tbl_13': tbl_13, 'tbl_14': tbl_14, 'tbl_15': tbl_15, 'tbl_16': tbl_16, 'tbl_17': tbl_17, 'tbl_18': tbl_18, 'tbl_19': tbl_19, 'tbl_20': tbl_20, 'tbl_21': tbl_21, 'tbl_22': tbl_22, 'tbl_23': tbl_23, 'tbl_24': tbl_24, 'tbl_25': tbl_25, 'tbl_26': tbl_26, 'tbl_27': tbl_27, 'tbl_28': tbl_28, 'tbl_29': tbl_29, 'tbl_30': tbl_30, 'tbl_31': tbl_31, 'W_top1': W_top1, 'b_top1': b_top1, 'W_top2': W_top2, 'b_top2': b_top2, 'W_top3': W_top3, 'L0_rec_kernel': _L0_rec_in['kernel'], 'L0_rec_W': _L0_rec_in['W'], 'L0_rec_b': _L0_rec_in['b']}

def reference(dense_ctx, ids, tbl_0, tbl_1, tbl_2, tbl_3, tbl_4, tbl_5, tbl_6, tbl_7, tbl_8, tbl_9, tbl_10, tbl_11, tbl_12, tbl_13, tbl_14, tbl_15, tbl_16, tbl_17, tbl_18, tbl_19, tbl_20, tbl_21, tbl_22, tbl_23, tbl_24, tbl_25, tbl_26, tbl_27, tbl_28, tbl_29, tbl_30, tbl_31, W_top1, b_top1, W_top2, b_top2, W_top3, L0_rec_kernel, L0_rec_W, L0_rec_b):
    import jax
    import jax.numpy as jnp

    def _L0_rec_ref(feat_emb, kernel, W, b):
        import jax, jax.numpy as jnp
        import numpy as np
        EMB_DIM = 64
        NUM_FIELDS = 32
        NUM_PAIRS = NUM_FIELDS * (NUM_FIELDS - 1) // 2
        D1 = 256
        BATCH = 256
        num_fields = feat_emb.shape[1]
        rows, cols = np.triu_indices(num_fields, k=1)
        p = feat_emb[:, rows, :]
        q = feat_emb[:, cols, :]
        pij = jnp.einsum('bpe,dpe,bpd->bp', p, kernel, q)
        return pij @ W.T + b
    e = jnp.stack([tbl_0[ids[:, 0]], tbl_1[ids[:, 1]], tbl_2[ids[:, 2]], tbl_3[ids[:, 3]], tbl_4[ids[:, 4]], tbl_5[ids[:, 5]], tbl_6[ids[:, 6]], tbl_7[ids[:, 7]], tbl_8[ids[:, 8]], tbl_9[ids[:, 9]], tbl_10[ids[:, 10]], tbl_11[ids[:, 11]], tbl_12[ids[:, 12]], tbl_13[ids[:, 13]], tbl_14[ids[:, 14]], tbl_15[ids[:, 15]], tbl_16[ids[:, 16]], tbl_17[ids[:, 17]], tbl_18[ids[:, 18]], tbl_19[ids[:, 19]], tbl_20[ids[:, 20]], tbl_21[ids[:, 21]], tbl_22[ids[:, 22]], tbl_23[ids[:, 23]], tbl_24[ids[:, 24]], tbl_25[ids[:, 25]], tbl_26[ids[:, 26]], tbl_27[ids[:, 27]], tbl_28[ids[:, 28]], tbl_29[ids[:, 29]], tbl_30[ids[:, 30]], tbl_31[ids[:, 31]]], axis=1)
    z = _L0_rec_ref(e, L0_rec_kernel, L0_rec_W, L0_rec_b)
    z = z.reshape(z.shape[0], -1)
    h = jnp.concatenate([z, dense_ctx], axis=1)
    h = jnp.maximum(h @ W_top1 + b_top1, 0.0)
    h = jnp.maximum(h @ W_top2 + b_top2, 0.0)
    y = h @ W_top3
    return y

_drawn_inputs = setup_inputs


def setup_inputs(seed=0):
    import zlib

    import numpy as np

    out = dict(_drawn_inputs(seed))
    spreads = {'b_top1': (0.0, 0.1), 'b_top2': (0.0, 0.1), 'L0_rec_b': (0.0, 0.1)}
    factors = {'tbl_0': 3.415,
     'tbl_1': 3.217,
     'tbl_2': 3.405,
     'tbl_3': 3.231,
     'tbl_4': 3.594,
     'tbl_5': 3.265,
     'tbl_6': 3.116,
     'tbl_7': 3.077,
     'tbl_8': 3.344,
     'tbl_9': 2.946,
     'tbl_10': 3.409,
     'tbl_11': 3.097,
     'tbl_12': 3.148,
     'tbl_13': 3.492,
     'tbl_14': 3.197,
     'tbl_15': 3.256,
     'tbl_16': 3.382,
     'tbl_17': 3.08,
     'tbl_18': 3.412,
     'tbl_19': 2.936,
     'tbl_20': 3.023,
     'tbl_21': 3.476,
     'tbl_22': 3.531,
     'tbl_23': 3.113,
     'tbl_24': 3.219,
     'tbl_25': 3.124,
     'tbl_26': 3.24,
     'tbl_27': 3.385,
     'tbl_28': 3.569,
     'tbl_29': 3.36,
     'tbl_30': 3.25,
     'tbl_31': 3.29}
    for name, (base, spread) in spreads.items():
        noise = np.random.default_rng([zlib.crc32(name.encode()), seed]).standard_normal(out[name].shape)
        drawn = base * np.exp(spread * noise) if base else spread * noise
        out[name] = jnp.asarray(drawn.astype(out[name].dtype))
    for name, factor in factors.items():
        out[name] = (out[name] * factor).astype(out[name].dtype)
    return out
```

```python
import numpy as np
import concourse.bass as bass
from concourse import mybir
from contextlib import ExitStack

F32 = mybir.dt.float32
F32R = mybir.dt.float32r
I32 = mybir.dt.int32
ALU = mybir.AluOpType
ACT = mybir.ActivationFunctionType

FIELDS, DIM, BATCH, DENSE = 32, 64, 1024, 16
P = 128
ROWS = 512
PASSES = BATCH // ROWS
BT = ROWS // P
BLOCKS = FIELDS // 2
UNITS = BLOCKS * BLOCKS
ITER = 16
CHUNKS = UNITS // ITER
BODY = 2 * ITER
BODIES = PASSES * UNITS // BODY
LAG = 3
TBANKS = 4
AHEAD = 5
XSLOTS = 8
SLOT_UNITS = 4
KSLOTS = BODY // SLOT_UNITS
PREP_AT = 8
C_OUT, H1, H2 = 256, 512, 256
KROWS = PASSES * UNITS
KC = KROWS // P


def pair_row_order():
    order = [None] * KROWS
    for n in range(BLOCKS):
        for u in range(2 * n + 1):
            unit = n * n + u
            k, v = unit // ITER, unit % ITER
            g, s = v % 4, v // 4
            j = 2 * n + 1 if u % 2 == 0 else 2 * n
            for half in range(2):
                i = 2 * (u // 2) + half
                if i < j:
                    order[32 * k + 8 * g + 2 * s + half] = (i, j)
    return order


def build(nc, dense_t, ids, tables, w_pair, b_pair, w1, b1, w2, b2, w3, kraw, ident_in, sel_in, out):
    k_scratch = nc.dram_tensor("k_split", (CHUNKS, 2, 2, DIM, 1024), F32, kind="Internal").ap()
    pij_scratch = nc.dram_tensor("pij_rows", (PASSES, KROWS, ROWS), F32, kind="Internal").ap()

    ctx = ExitStack()
    with ctx:
        def sb(name, shape, dt=F32):
            return ctx.enter_context(nc.sbuf_tensor(name, shape, dt))

        def sem(name):
            return ctx.enter_context(nc.semaphore(name))

        xt = sb("xt", [P, PASSES * BLOCKS * ROWS])
        xr = sb("xr", [P, XSLOTS * 4 * ROWS], F32R)
        gathered = [sb(f"gathered{i}", [P, BT, P]) for i in range(2)]
        xsplit = [sb(f"xsplit{i}", [P, 2, ROWS], F32R) for i in range(2)]
        kslot = [sb(f"kslot{i}", [P, SLOT_UNITS, P], F32R) for i in range(KSLOTS)]
        ksplit = [sb(f"ksplit{i}", [P, 2, 1024]) for i in range(2)]
        prod = [sb(f"prod{i}", [P, ROWS]) for i in range(TBANKS)]
        pij_sb = [sb(f"pij_sb{i}", [P, ROWS]) for i in range(2)]
        ident = sb("ident", [P, P])
        sel = sb("sel", [P, 4, 32])
        idx = sb("idx", [P, BATCH // P, FIELDS], I32)

        at = [0]

        def reuse(rows, cols):
            a = at[0]
            at[0] += cols
            assert at[0] <= BLOCKS * ROWS
            return xt[0:rows, a:a + cols]

        wp_sb = reuse(P, KC * C_OUT).rearrange("p (c n) -> p c n", c=KC)
        w1_sb = reuse(P, 2 * H1).rearrange("p (c n) -> p c n", c=2)
        w1d_sb = reuse(DENSE, H1)
        w2_sb = reuse(P, 4 * H2).rearrange("p (c n) -> p c n", c=4)
        w3_sb = reuse(P, 2)
        bp_sb = reuse(P, 2)
        b1_sb = reuse(P, 4)
        b2_sb = reuse(P, 2)
        dense_sb = reuse(DENSE, BATCH)
        TOWER_LOADS = 9
        pij_all = [xr[:, p * KC * ROWS:(p + 1) * KC * ROWS].bitcast(F32).rearrange("p (c n) -> p c n", c=KC)
                   for p in range(PASSES)]
        z_sb = [xt[:, (16 + 2 * p) * ROWS:(18 + 2 * p) * ROWS].rearrange("p (c n) -> p c n", c=2) for p in range(PASSES)]
        h1_sb = [xt[:, (20 + 4 * p) * ROWS:(24 + 4 * p) * ROWS].rearrange("p (c n) -> p c n", c=4) for p in range(PASSES)]
        h2_sb = [xt[:, (28 + 2 * p) * ROWS:(30 + 2 * p) * ROWS].rearrange("p (c n) -> p c n", c=2) for p in range(PASSES)]
        y_sb = ksplit[0][0:1, 0, 0:BATCH]

        bank = [ctx.enter_context(nc.psum_tensor(f"bank{i}", [P, ROWS], F32)) for i in range(8)]
        t_ps = bank[0:4]
        acc = bank[4:6]
        tp_ps = bank[6:8]

        consts_in = sem("consts_in")
        idx_in = sem("idx_in")
        block_in = [sem(f"block_in{i}") for i in range(2)]
        transposed = sem("transposed")
        x_hi_done = sem("x_hi_done")
        x_lo_done = sem("x_lo_done")
        x_ready = sem("x_ready")
        kraw_in = [sem(f"kraw_in{i}") for i in range(2)]
        k_hi_done = sem("k_hi_done")
        k_lo_done = sem("k_lo_done")
        k_stored = [sem(f"k_stored{i}") for i in range(2)]
        kslot_in = [sem(f"kslot_in{i}") for i in range(KSLOTS)]
        t_ready = sem("t_ready")
        prod_ready = sem("prod_ready")
        prod_used = sem("prod_used")
        pij_ready = sem("pij_ready")
        pij_stored = [sem(f"pij_stored{i}") for i in range(2)]
        tower_in = sem("tower_in")
        pij_in = [sem(f"pij_in{i}") for i in range(PASSES)]
        mm_done = sem("mm_done")
        act_done = sem("act_done")
        out_done = sem("out_done")

        block = ctx.enter_context(nc.Block())

        def unit_registers(e, name):
            u, top, t, a, b = (e.alloc_register(f"{name}_{x}") for x in ("u", "top", "t", "a", "b"))
            e.reg_mov(u, 0)
            e.reg_mov(top, 0)

            def advance():
                e.reg_alu(u, u, 1, ALU.add)
                e.reg_alu(t, top, 2 * BLOCKS - 1, ALU.bitwise_and)
                e.reg_alu(a, u, t, ALU.is_gt)
                e.reg_alu(t, a, 1, ALU.logical_shift_left)
                e.reg_alu(top, top, t, ALU.add)
                e.reg_alu(t, u, a, ALU.mult)
                e.reg_alu(u, u, t, ALU.subtract)

            def xr_offset():
                e.reg_alu(a, top, XSLOTS * 2 - 1, ALU.bitwise_and)
                e.reg_alu(a, a, 2 * ROWS, ALU.mult)
                e.reg_alu(b, u, 1, ALU.bitwise_and)
                e.reg_alu(b, b, -2 * ROWS, ALU.mult)
                e.reg_alu(a, a, b, ALU.add)
                return e.snap(a, min_val=-2 * ROWS, max_val=(XSLOTS * 4 - 4) * ROWS) + 2 * ROWS

            def xt_offset():
                e.reg_alu(a, top, 5, ALU.logical_shift_right)
                e.reg_alu(a, a, 5, ALU.logical_shift_left)
                e.reg_alu(a, a, u, ALU.add)
                e.reg_alu(a, a, 1, ALU.logical_shift_right)
                e.reg_alu(a, a, ROWS, ALU.mult)
                return e.snap(a, min_val=0, max_val=(PASSES * BLOCKS - 1) * ROWS)

            return advance, xr_offset, xt_offset

        def bodies(e, body, change=()):
            starts = sorted({0, *change, BODIES - 3})
            for lo, hi in zip(starts, starts[1:]):
                with e.Fori(lo, hi) as b:
                    body(b, lo)
            for b in range(BODIES - 3, BODIES):
                body(b, b)

        def block_of(B, h):
            return B * 2 + (h + AHEAD)

        def prepares(at, h):
            return 2 * at + h + AHEAD < PASSES * BLOCKS

        @block.sync
        def _(sp):
            sp.dma_start(idx[:], ids.rearrange("(t p) f -> p t f", p=P)).then_inc(idx_in, 16)
            sp.dma_start(ident[:], ident_in).then_inc(consts_in, 16)
            sp.dma_start(sel[:], sel_in).then_inc(consts_in, 16)

            def load_raw(c, s):
                sp.dma_start(ksplit[s][:, 1, :], kraw[c, :, :]).then_inc(kraw_in[s], 16)

            def store_split(c, s):
                for a in range(2):
                    sp.dma_start(k_scratch[c, a, :, :, :].rearrange("s d x -> d s x"),
                                 ksplit[s][64 * a:64 * a + 64, :, :]).then_inc(k_stored[s], 16)

            def load_slot(c, h, q):
                slot = h * 4 + q
                src = k_scratch[c, q // 2, :, :, (q % 2) * 512:(q % 2) * 512 + 512]
                sp.dma_start(kslot[slot][:].rearrange("p u n -> p (u n)").bitcast(F32),
                             src.rearrange("s d x -> (s d) x")).then_inc(kslot_in[slot], 16)

            load_raw(0, 0)
            load_raw(1, 1)
            for c in range(4):
                sp.wait_ge(k_lo_done, c + 1)
                store_split(c, c % 2)
                sp.wait_ge(k_stored[c % 2], 32 * (c // 2 + 1))
                load_raw(c + 2, c % 2)
                if c < 2:
                    for q in range(4):
                        load_slot(c, c, q)

            def body(B, at):
                for h in range(2):
                    for q in range(4):
                        if at < BODIES - 1:
                            sp.wait_ge(t_ready, B * BODY + (h * ITER + 4 * q + 4))
                            if at < 7:
                                load_slot(B * 2 + (2 + h), h, q)
                            elif isinstance(at, int) and at == 7:
                                load_slot(B * 2 + (2 + h - CHUNKS), h, q)
                            else:
                                load_slot(B * 2 + (2 + h - CHUNKS), h, q)
                        if q == 1 and at < 6:
                            sp.wait_ge(k_lo_done, B * 2 + (5 + h))
                            store_split(B * 2 + (4 + h), h)
                            sp.wait_ge(k_stored[h], B * 32 + 96)
                            if at < 5:
                                load_raw(B * 2 + (6 + h), h)
                    if at == BODIES - 3 and h == 0:
                        load_tower()
                    sp.wait_ge(pij_ready, B * 2 + (h + 1))
                    store_pij(B, at, h)

            def store_pij(B, at, h):
                p = 0 if at < 8 else 1
                for g in range(4):
                    row = B * 64 + (32 * h + 8 * g - p * KROWS)
                    sp.dma_start(pij_scratch[p, bass.ds(row, 8), :], pij_sb[h][32 * g:32 * g + 8, :])\
                      .then_inc(pij_stored[h], 16)

            def load_tower():
                sp.wait_ge(prod_ready, UNITS)
                for dst, src in ((wp_sb, w_pair.rearrange("(c p) n -> p c n", p=P)),
                                 (w1_sb, w1[0:C_OUT, :].rearrange("(c p) n -> p c n", p=P)),
                                 (w1d_sb, w1[C_OUT:C_OUT + DENSE, :]),
                                 (w2_sb, w2.rearrange("(c p) n -> p c n", p=P)),
                                 (w3_sb, w3), (bp_sb, b_pair), (b1_sb, b1), (b2_sb, b2), (dense_sb, dense_t)):
                    sp.dma_start(dst, src).then_inc(tower_in, 16)

            bodies(sp, body, change=(5, 6, 7, 8))

            for h in range(2):
                sp.wait_ge(pij_stored[h], 64 * BODIES)
            sp.wait_ge(t_ready, PASSES * UNITS)
            for p in range(PASSES):
                sp.dma_start(pij_all[p], pij_scratch[p, :, :].rearrange("(c p) n -> p c n", p=P))\
                  .then_inc(pij_in[p], 16)
            sp.wait_ge(act_done, 2 * (2 + 4 + 2 + 1))
            sp.dma_start(out, y_sb).then_inc(out_done, 16)
            sp.wait_ge(out_done, 16)

        @block.gpsimd
        def _(pool):
            pool.wait_ge(idx_in, 16)
            for b in range(PASSES * BLOCKS):
                p, n = b // BLOCKS, b % BLOCKS
                if b >= 2:
                    pool.wait_ge(transposed, b - 1)
                for t in range(BT):
                    for half in range(2):
                        f = 2 * n + half
                        pool.indirect_dma_start(
                            out=gathered[b % 2][:, t, DIM * half:DIM * half + DIM], out_offset=None,
                            in_=tables[f],
                            in_offset=bass.IndirectOffsetOnAxis(ap=idx[:, p * BT + t, f:f + 1], axis=0),
                        ).then_inc(block_in[b % 2], 16)

        @block.tensor
        def _(pe):
            advance, xr_offset, _ = unit_registers(pe, "pe")

            def transpose_block(b, slot, landed, hi_before):
                pe.wait_ge(block_in[slot], landed)
                if hi_before is not None:
                    pe.wait_ge(x_hi_done, hi_before)
                for t in range(BT):
                    mm = pe.transpose(tp_ps[slot][:, t * P:t * P + P], gathered[slot][:, t, :], ident[:])
                mm.then_inc(transposed, 1)

            def products(v):
                off = xr_offset()
                w = kslot[v // SLOT_UNITS][:, v % SLOT_UNITS, :]
                pe.matmul(t_ps[v % TBANKS][:], w, xr[:, bass.ds(off, ROWS)], start=True, stop=False)
                pe.matmul(t_ps[v % TBANKS][:], w, xr[:, bass.ds(off + ROWS, ROWS)], start=False, stop=True)\
                  .then_inc(t_ready, 1)
                advance()

            def sum_over_e(v):
                g, s = v % 4, v % ITER // 4
                pe.matmul(acc[v // ITER][32 * g:32 * g + 32, :], sel[:, s, :], prod[v % TBANKS][:],
                          start=(s == 0), stop=(s == 3)).then_inc(prod_used, 1)

            pe.wait_ge(consts_in, 32)
            for b in range(AHEAD):
                transpose_block(b, b % 2, P * (b // 2 + 1), b - 1 if b >= 2 else None)
            pe.wait_ge(kslot_in[0], 16)
            pe.wait_ge(x_ready, 2)
            for v in range(LAG):
                products(v)

            def body(B, at):
                for v in range(BODY):
                    h, r = v // ITER, v % ITER
                    ahead = v + LAG
                    if not (at == BODIES - 1 and ahead >= BODY):
                        if ahead % SLOT_UNITS == 0:
                            pe.wait_ge(kslot_in[ahead % BODY // SLOT_UNITS], B * 16 + (16 if ahead < BODY else 32))
                        if r == ITER - LAG or v == 0 and at == 0:
                            nxt = h + (1 if r == ITER - LAG else 0)
                            pe.wait_ge(x_ready, B * 2 + (nxt + AHEAD) if at < BODIES - 3 else
                                       min(2 * B + nxt + AHEAD, PASSES * BLOCKS))
                        products(ahead % BODY)
                    if r == 0:
                        pe.wait_ge(pij_ready, B * 2 + (h - 1)) if at > 0 else None
                    pe.wait_ge(prod_ready, B * BODY + (v + 1))
                    sum_over_e(v)
                    if r == PREP_AT and prepares(at, h):
                        b = block_of(B, h)
                        transpose_block(b, (h + AHEAD) % 2, B * P + P * ((h + AHEAD) // 2 + 1), b - 1)

            bodies(pe, body, change=(1,))

            banks = [0]

            def tower(p, m_rows, terms, stop_inc=True):
                n = banks[0]
                banks[0] += 1
                if n >= 8:
                    pe.wait_ge(act_done, n - 7)
                for k, (w, x) in enumerate(terms):
                    mm = pe.matmul(bank[n % 8][0:m_rows, :], w, x, start=(k == 0), stop=(k == len(terms) - 1))
                mm.then_inc(mm_done, 1)

            pe.wait_ge(tower_in, 16 * TOWER_LOADS)
            pe.wait_ge(pij_ready, 2 * BODIES)
            for p in range(PASSES):
                pe.wait_ge(pij_in[p], 16)
                for m in range(2):
                    tower(p, P, [(wp_sb[:, c, P * m:P * m + P], pij_all[p][:, c, :]) for c in range(KC)])
            for p in range(PASSES):
                pe.wait_ge(act_done, 2 * p + 2)
                for m in range(4):
                    tower(p, P, [(w1_sb[:, c, P * m:P * m + P], z_sb[p][:, c, :]) for c in range(2)]
                          + [(w1d_sb[:, P * m:P * m + P], dense_sb[:, p * ROWS:(p + 1) * ROWS])])
            for p in range(PASSES):
                pe.wait_ge(act_done, 4 + 4 * p + 4)
                for m in range(2):
                    tower(p, P, [(w2_sb[:, c, P * m:P * m + P], h1_sb[p][:, c, :]) for c in range(4)])
            for p in range(PASSES):
                pe.wait_ge(act_done, 12 + 2 * p + 2)
                tower(p, 1, [(w3_sb[:, c:c + 1], h2_sb[p][:, c, :]) for c in range(2)])

        @block.vector
        def _(dve):
            advance, _, xt_offset = unit_registers(dve, "dve")

            def split_k(c, s):
                dve.wait_ge(k_hi_done, c + 1)
                nc.vector.tensor_tensor(ksplit[s][:, 1, :].bitcast(F32R), ksplit[s][:, 1, :], ksplit[s][:, 0, :],
                                        ALU.subtract).then_inc(k_lo_done, 1)

            def split_x(b, s):
                dve.wait_ge(x_hi_done, b + 1)
                nc.vector.tensor_tensor(xsplit[s][:, 1, :], xt[:, bass.ds(b * ROWS, ROWS)],
                                        xsplit[s][:, 0, :].bitcast(F32), ALU.subtract).then_inc(x_lo_done, 1)

            def multiply(B, v):
                off = xt_offset()
                advance()
                dve.wait_ge(t_ready, B * BODY + (v + 1))
                if not (isinstance(B, int) and B == 0 and v < TBANKS):
                    dve.wait_ge(prod_used, B * BODY + (v + 1 - TBANKS))
                nc.vector.tensor_tensor(prod[v % TBANKS][:], t_ps[v % TBANKS][:], xt[:, bass.ds(off, ROWS)],
                                        ALU.mult).then_inc(prod_ready, 1)

            split_k(0, 0)
            split_k(1, 1)
            split_x(0, 0)
            split_k(2, 0)
            split_k(3, 1)
            for b in range(1, AHEAD):
                split_x(b, b % 2)

            def body(B, at):
                for h in range(2):
                    for r in range(ITER):
                        multiply(0 if at == 0 else B, h * ITER + r)
                        if r == 1 and at < 6:
                            split_k(B * 2 + (4 + h), h)
                        if r == PREP_AT + 2 and prepares(at, h):
                            split_x(block_of(B, h), (h + AHEAD) % 2)

            bodies(dve, body, change=(1, 6))

        @block.scalar
        def _(act):
            def copy(dst, src):
                return nc.scalar.activation(dst, src, ACT.Copy)

            def round_k(c, s, landed):
                act.wait_ge(kraw_in[s], landed)
                copy(ksplit[s][:, 0, :].bitcast(F32R), ksplit[s][:, 1, :]).then_inc(k_hi_done, 1)

            def prepare_x(b, s):
                act.wait_ge(transposed, b + 1)
                copy(xsplit[s][:, 0, :], tp_ps[s][:])
                copy(xt[:, bass.ds(b * ROWS, ROWS)], tp_ps[s][:]).then_inc(x_hi_done, 1)
                act.wait_ge(x_hi_done, b + 1)
                act.wait_ge(x_lo_done, b + 1)
                for f in range(2):
                    for half in range(2):
                        base = (b % XSLOTS) * (4 * ROWS) + 2 * ROWS * f
                        last = copy(xr[64 * half:64 * half + 64, bass.ds(base, 2 * ROWS)],
                                    xsplit[s][64 * f:64 * f + 64, :, :].rearrange("p s n -> p (s n)").bitcast(F32))
                last.then_inc(x_ready, 1)

            round_k(0, 0, 16)
            round_k(1, 1, 16)
            prepare_x(0, 0)
            round_k(2, 0, 32)
            round_k(3, 1, 32)
            for b in range(1, AHEAD):
                prepare_x(b, b % 2)

            def body(B, at):
                for h in range(2):
                    if at < 6:
                        round_k(B * 2 + (4 + h), h, B * 16 + 48)
                    if prepares(at, h):
                        prepare_x(block_of(B, h), (h + AHEAD) % 2)
                    if at > 0:
                        act.wait_ge(pij_stored[h], B * 64)
                    act.wait_ge(prod_used, B * BODY + (h * ITER + ITER))
                    copy(pij_sb[h][:], acc[h][:]).then_inc(pij_ready, 1)

            bodies(act, body, change=(1, 6))

            done = [0]

            def finish(dst, rows, func, bias):
                n = done[0]
                done[0] += 1
                act.wait_ge(mm_done, n + 1)
                if bias is None:
                    copy(dst, bank[n % 8][0:rows, :]).then_inc(act_done, 1)
                else:
                    nc.scalar.activation(dst, bank[n % 8][0:rows, :], func, bias=bias).then_inc(act_done, 1)

            act.wait_ge(tower_in, 16 * TOWER_LOADS)
            for p in range(PASSES):
                for m in range(2):
                    finish(z_sb[p][:, m, :], P, ACT.Identity, bp_sb[:, m:m + 1])
            for p in range(PASSES):
                for m in range(4):
                    finish(h1_sb[p][:, m, :], P, ACT.Relu, b1_sb[:, m:m + 1])
            for p in range(PASSES):
                for m in range(2):
                    finish(h2_sb[p][:, m, :], P, ACT.Relu, b2_sb[:, m:m + 1])
            for p in range(PASSES):
                finish(y_sb[:, p * ROWS:(p + 1) * ROWS], 1, None, None)


def lay_out(inputs):
    a = {k: np.asarray(v) for k, v in inputs.items()}
    rows, cols = np.triu_indices(FIELDS, k=1)
    number = {(int(i), int(j)): p for p, (i, j) in enumerate(zip(rows, cols))}
    k_in = a["L0_rec_kernel"]
    kraw = np.zeros((CHUNKS, 2, DIM, ITER // 2, 2, DIM), k_in.dtype)
    for n in range(BLOCKS):
        for u in range(2 * n + 1):
            unit = n * n + u
            c, v = unit // ITER, unit % ITER
            j = 2 * n + 1 if u % 2 == 0 else 2 * n
            for half in range(2):
                i = 2 * (u // 2) + half
                if i < j:
                    kraw[c, v // 8, :, v % 8, half, :] = k_in[:, number[i, j], :]
    w = a["L0_rec_W"]
    w_pair = np.zeros((KROWS, C_OUT), w.dtype)
    for row, pair in enumerate(pair_row_order()):
        if pair is not None:
            w_pair[row, :] = w[:, number[pair]]
    sel = np.zeros((P, 4, 32), np.float32)
    for s in range(4):
        sel[0:64, s, 2 * s] = 1.0
        sel[64:128, s, 2 * s + 1] = 1.0

    def columns(x):
        return np.ascontiguousarray(x.reshape(-1, P).T)

    return {
        "dense_t": np.ascontiguousarray(a["dense_ctx"].T), "ids": a["ids"],
        **{f"tbl_{f}": a[f"tbl_{f}"] for f in range(FIELDS)},
        "w_pair": w_pair, "b_pair": columns(a["L0_rec_b"]),
        "w1": a["W_top1"], "b1": columns(a["b_top1"]), "w2": a["W_top2"], "b2": columns(a["b_top2"]),
        "w3": columns(a["W_top3"]), "kraw": kraw.reshape(CHUNKS, P, 1024),
        "ident": np.eye(P, dtype=np.float32), "sel": sel,
    }


def kernel(**inputs):
    import concourse.bacc as bacc
    from concourse.bass_utils import run_bass_kernel_spmd

    arrays = {f"{k}_dram": np.ascontiguousarray(v) for k, v in lay_out(inputs).items()}
    nc = bacc.Bacc("TRN2", target_bir_lowering=False, num_devices=1)
    d = {k[:-5]: nc.dram_tensor(k, v.shape, mybir.dt.from_np(v.dtype), kind="ExternalInput").ap()
         for k, v in arrays.items()}
    out = nc.dram_tensor("y_dram", (1, BATCH), F32, kind="ExternalOutput").ap()
    build(nc, d["dense_t"], d["ids"], [d[f"tbl_{f}"] for f in range(FIELDS)], d["w_pair"], d["b_pair"], d["w1"],
          d["b1"], d["w2"], d["b2"], d["w3"], d["kraw"], d["ident"], d["sel"], out)
    r = run_bass_kernel_spmd(nc, [arrays], core_ids=[0])
    return np.asarray(r.results[0]["y_dram"]).reshape(BATCH, 1)
```

```python
import numpy as np
import concourse.bass as bass
from concourse import mybir
from contextlib import ExitStack

F32 = mybir.dt.float32
F32R = mybir.dt.float32r
I32 = mybir.dt.int32
ALU = mybir.AluOpType
ACT = mybir.ActivationFunctionType

FIELDS, DIM, BATCH, DENSE = 32, 64, 1024, 16
P = 128
ROWS = 512
PASSES = BATCH // ROWS
BT = ROWS // P
BLOCKS = FIELDS // 2
NBLOCKS = PASSES * BLOCKS
UNITS = BLOCKS * BLOCKS
STEPS = UNITS // 2
NSTEPS = PASSES * STEPS
CHUNK = 16
CHUNKS = UNITS // CHUNK
SLOT_UNITS = 4
KSLOTS = 8
BUFS = 3
LAG = 2
AHEAD = 5
K_AHEAD = 10
XSLOTS = 6
Q_UNITS = 64
QUARTERS = UNITS // Q_UNITS
C_OUT, H1, H2 = 256, 512, 256
PAIR_ROWS = QUARTERS * P


def pass_units():
    units = []
    for n in range(BLOCKS):
        if n % 2:
            units += [(2 * n - 1, n - 1), (2 * n + 1, n)]
        for m in range(n):
            units += [(2 * n + 1, m), (2 * n, m)]
    return units


PASS_UNITS = pass_units()


def unit_pairs(unit):
    j, m = unit
    return [(i, j) if i < j else None for i in (2 * m, 2 * m + 1)]


def pij_row(w, half):
    q, v = w // Q_UNITS, w % Q_UNITS
    return P * q + 32 * (v % 4) + 2 * (v // 4) + half


def step_block(s):
    j = max(PASS_UNITS[2 * (s % STEPS)][0], PASS_UNITS[2 * (s % STEPS) + 1][0])
    return s // STEPS * BLOCKS + j // 2


def startup_order():
    items = [(8.4 * b + 13.0, "x", b) for b in range(AHEAD)] + [(3.5 * c + 6.0, "k", c) for c in range(K_AHEAD)]
    return [(kind, n) for _, kind, n in sorted(items)]


BLOCK_AT = {(CHUNK * (b - AHEAD) + 4) // 2: b for b in range(AHEAD, NBLOCKS)}
CHUNK_AT = {8 * (c - K_AHEAD) + 5: c for c in range(K_AHEAD, CHUNKS)}


def build(nc, dense_t, ids, tables, w_pair, b_pair, w1, b1, w2, b2, w3, kraw, ident_in, sel_in, out):
    k_scratch = nc.dram_tensor("k_split", (CHUNKS, 2, 2, DIM, 1024), F32, kind="Internal").ap()

    ctx = ExitStack()
    with ctx:
        def sb(name, shape, dt=F32):
            return ctx.enter_context(nc.sbuf_tensor(name, shape, dt))

        def sem(name):
            return ctx.enter_context(nc.semaphore(name))

        xt = sb("xt", [P, NBLOCKS * ROWS])
        xr = sb("xr", [P, XSLOTS, 2, 2, ROWS], F32R)
        gathered = [sb(f"gathered{i}", [P, BT, P]) for i in range(2)]
        xsplit = [sb(f"xsplit{i}", [P, 2, ROWS], F32R) for i in range(2)]
        kslot = [sb(f"kslot{i}", [P, SLOT_UNITS, P], F32R) for i in range(KSLOTS)]
        ksplit = [sb(f"ksplit{i}", [P, 2, 1024]) for i in range(2)]
        prod = sb("prod", [P, BUFS, 2, ROWS])
        pij_sb = [sb(f"pij{p}", [P, QUARTERS, ROWS]) for p in range(PASSES)]
        w_eff = sb("w_eff", [P, QUARTERS, H1])
        b_eff = sb("b_eff", [P, H1 // P])
        b1_sb = sb("b1_sb", [P, H1 // P])
        bp_sb = sb("bp_sb", [P, C_OUT // P])
        ident = sb("ident", [P, P])
        sel = sb("sel", [P, 62])
        idx = sb("idx", [P, BATCH // P, FIELDS], I32)

        def part_of(start, rows, cols):
            return xt[0:rows, start:start + cols], start + cols

        second = BLOCKS * ROWS
        wp_sb, at = part_of(second, P, 2 * PAIR_ROWS)
        w1_sb, at = part_of(at, P, 2 * H1)
        wp_sb = wp_sb.rearrange("p (c n) -> p c n", c=2)
        w1_sb = w1_sb.rearrange("p (c n) -> p c n", c=2)
        assert at <= second + 4 * ROWS
        w1d_sb, at = part_of(0, DENSE, H1)
        w2_sb, at = part_of(at, P, 4 * H2)
        w2_sb = w2_sb.rearrange("p (c n) -> p c n", c=4)
        w3_sb, at = part_of(at, P, 2)
        b2_sb, at = part_of(at, P, 2)
        dense_sb, at = part_of(at, DENSE, BATCH)
        assert at <= second
        TOWER_LOADS = 5
        h1_sb = [xt[:, second + 4 * p * ROWS:second + 4 * (p + 1) * ROWS].rearrange("p (c n) -> p c n", c=4)
                 for p in range(PASSES)]
        h2_sb = [xt[:, second + (8 + 2 * p) * ROWS:second + (10 + 2 * p) * ROWS].rearrange("p (c n) -> p c n", c=2)
                 for p in range(PASSES)]
        y_sb = ksplit[0][0:1, 0, 0:BATCH]

        t_ps = ctx.enter_context(nc.psum_tensor("t_ps", [P, BUFS, 2, ROWS], F32))
        acc = ctx.enter_context(nc.psum_tensor("acc", [P, ROWS], F32))
        tp = ctx.enter_context(nc.psum_tensor("tp", [P, ROWS], F32))
        banks = [t_ps[:, i // 2, i % 2, :] for i in range(2 * BUFS)]

        consts_in = sem("consts_in")
        idx_in = sem("idx_in")
        w_in = sem("w_in")
        block_in = [sem(f"block_in{i}") for i in range(2)]
        transposed = sem("transposed")
        x_hi_done = sem("x_hi_done")
        x_lo_done = sem("x_lo_done")
        x_ready = sem("x_ready")
        kraw_in = [sem(f"kraw_in{i}") for i in range(2)]
        k_hi_done = sem("k_hi_done")
        k_lo_done = sem("k_lo_done")
        k_stored = [sem(f"k_stored{i}") for i in range(2)]
        kslot_in = [sem(f"kslot_in{i}") for i in range(KSLOTS)]
        t_ready = sem("t_ready")
        prod_ready = sem("prod_ready")
        prod_used = sem("prod_used")
        pij_ready = sem("pij_ready")
        w_eff_mm = sem("w_eff_mm")
        w_eff_done = sem("w_eff_done")
        tower_in = sem("tower_in")
        mm_done = sem("mm_done")
        act_done = sem("act_done")
        out_done = sem("out_done")

        block = ctx.enter_context(nc.Block())

        @block.sync
        def _(sp):
            def load_raw(c):
                sp.dma_start(ksplit[c % 2][:, 1, :], kraw[c, :, :]).then_inc(kraw_in[c % 2], 16)

            def store_split(c):
                sp.wait_ge(k_lo_done, c + 1)
                for a in range(2):
                    sp.dma_start(k_scratch[c, a, :, :, :].rearrange("s d x -> d s x"),
                                 ksplit[c % 2][64 * a:64 * a + 64, :, :]).then_inc(k_stored[c % 2], 16)

            def load_next_raw(c):
                sp.wait_ge(k_stored[c % 2], 32 * (c // 2 + 1))
                if c + 2 < CHUNKS:
                    load_raw(c + 2)

            def load_slot(w):
                c, v = w % UNITS // CHUNK, w % CHUNK
                src = k_scratch[c, v // 8, :, :, P * (v % 8):P * (v % 8 + SLOT_UNITS)]
                slot = w // SLOT_UNITS % KSLOTS
                sp.dma_start(kslot[slot][:].rearrange("p u n -> p (u n)").bitcast(F32),
                             src.rearrange("s d x -> (s d) x")).then_inc(kslot_in[slot], 16)

            sp.dma_start(idx[:], ids.rearrange("(t p) f -> p t f", p=P)).then_inc(idx_in, 16)
            load_raw(0)
            load_raw(1)
            sp.dma_start(ident[:], ident_in).then_inc(consts_in, 16)
            sp.dma_start(sel[:], sel_in).then_inc(consts_in, 16)
            for dst, src in ((wp_sb, w_pair.rearrange("(c p) n -> p c n", p=P)),
                             (w1_sb, w1[0:C_OUT, :].rearrange("(c p) n -> p c n", p=P)),
                             (bp_sb[:], b_pair), (b1_sb[:], b1)):
                sp.dma_start(dst, src).then_inc(w_in, 16)
            for c in range(K_AHEAD):
                store_split(c)
                load_next_raw(c)
                if c < 2:
                    for w in range(CHUNK * c, CHUNK * (c + 1), SLOT_UNITS):
                        load_slot(w)

            for s in range(NSTEPS):
                w = 2 * s
                if w % SLOT_UNITS == 2 and w + 2 + (KSLOTS - 1) * SLOT_UNITS < PASSES * UNITS:
                    sp.wait_ge(t_ready, s + 1)
                    load_slot(w - 2 + KSLOTS * SLOT_UNITS)
                if s - 2 in CHUNK_AT:
                    store_split(CHUNK_AT[s - 2])
                if s - 4 in CHUNK_AT:
                    load_next_raw(CHUNK_AT[s - 4])
                if s == STEPS + 8:
                    sp.wait_ge(prod_ready, STEPS)
                    for dst, src in ((w1d_sb, w1[C_OUT:C_OUT + DENSE, :]),
                                     (w2_sb, w2.rearrange("(c p) n -> p c n", p=P)),
                                     (w3_sb, w3), (b2_sb, b2), (dense_sb, dense_t)):
                        sp.dma_start(dst, src).then_inc(tower_in, 16)

            sp.wait_ge(act_done, PASSES * (4 + 2 + 1))
            sp.dma_start(out, y_sb).then_inc(out_done, 16)
            sp.wait_ge(out_done, 16)

        @block.gpsimd
        def _(pool):
            def split_x(b):
                pool.wait_ge(x_hi_done, b + 1)
                nc.gpsimd.tensor_tensor(xsplit[b % 2][:, 1, :], xt[:, b * ROWS:(b + 1) * ROWS],
                                        xsplit[b % 2][:, 0, :].bitcast(F32), ALU.subtract).then_inc(x_lo_done, 1)

            pool.wait_ge(idx_in, 16)
            for b in range(NBLOCKS):
                p, n = b // BLOCKS, b % BLOCKS
                if b >= 2:
                    pool.wait_ge(transposed, b - 1)
                if b - 2 >= BLOCKS:
                    split_x(b - 2)
                for t in range(BT):
                    for half in range(2):
                        f = 2 * n + half
                        pool.indirect_dma_start(
                            out=gathered[b % 2][:, t, DIM * half:DIM * (half + 1)], out_offset=None,
                            in_=tables[f],
                            in_offset=bass.IndirectOffsetOnAxis(ap=idx[:, p * BT + t, f:f + 1], axis=0),
                        ).then_inc(block_in[b % 2], 16)
            split_x(NBLOCKS - 2)
            split_x(NBLOCKS - 1)

        @block.tensor
        def _(pe):
            def transpose_block(b):
                pe.wait_ge(block_in[b % 2], P * (b // 2 + 1))
                if b:
                    pe.wait_ge(x_hi_done, b)
                for t in range(BT):
                    mm = pe.transpose(tp[:, t * P:(t + 1) * P], gathered[b % 2][:, t, :], ident[:])
                mm.then_inc(transposed, 1)

            def fold_weights():
                pe.wait_ge(w_in, 64)
                for m in range(QUARTERS):
                    for c in range(2):
                        pe.matmul(banks[m], wp_sb[:, c, P * m:P * (m + 1)], w1_sb[:, c, :],
                                  start=(c == 0), stop=(c == 1))
                for m in range(H1 // P):
                    for c in range(2):
                        mm = pe.matmul(banks[4][:, m:m + 1], w1_sb[:, c, P * m:P * (m + 1)], bp_sb[:, c:c + 1],
                                       start=(c == 0), stop=(c == 1))
                mm.then_inc(w_eff_mm, 1)

            block_seen = [-1]

            def products(s):
                need = step_block(s)
                for h in range(2):
                    w = 2 * s + h
                    j, m = PASS_UNITS[w % UNITS]
                    b = w // UNITS * BLOCKS + j // 2
                    if w % SLOT_UNITS == 0:
                        pe.wait_ge(kslot_in[w // SLOT_UNITS % KSLOTS], 16 * (w // (SLOT_UNITS * KSLOTS) + 1))
                    if b > block_seen[0] or (need == b and j % 2 == 0):
                        pe.wait_ge(x_ready, 2 * b + (1 if j % 2 else 2))
                        block_seen[0] = max(b, block_seen[0])
                    weights = kslot[w // SLOT_UNITS % KSLOTS][:, w % SLOT_UNITS, :]
                    for part in range(2):
                        mm = pe.matmul(t_ps[:, s % BUFS, h, :], weights, xr[:, b % XSLOTS, j % 2, part, :],
                                       start=(part == 0), stop=(part == 1))
                mm.then_inc(t_ready, 1)

            def sum_over_e(s):
                pe.wait_ge(prod_ready, s + 1)
                for h in range(2):
                    v = (2 * s + h) % Q_UNITS
                    g, k = v % 4, v // 4
                    mm = pe.matmul(acc[32 * g:32 * g + 32, :], sel[:, 30 - 2 * k:62 - 2 * k], prod[:, s % BUFS, h, :],
                                   start=(k == 0), stop=(k == Q_UNITS // 4 - 1))
                mm.then_inc(prod_used, 1)

            pe.wait_ge(consts_in, 32)
            for b in range(AHEAD):
                transpose_block(b)
                if b == 2:
                    fold_weights()
            pe.wait_ge(w_eff_done, 1)
            for s in range(LAG):
                products(s)
            for s in range(NSTEPS):
                if s + LAG < NSTEPS:
                    products(s + LAG)
                if s and 2 * s % Q_UNITS == 0:
                    pe.wait_ge(pij_ready, 2 * s // Q_UNITS)
                sum_over_e(s)
                if s in BLOCK_AT:
                    transpose_block(BLOCK_AT[s])

            count = [0]

            def layer_bank(rows, terms):
                n = count[0]
                count[0] += 1
                if n >= len(banks):
                    pe.wait_ge(act_done, n - len(banks) + 1)
                for k, (w, x) in enumerate(terms):
                    mm = pe.matmul(banks[n % len(banks)][0:rows, :], w, x, start=(k == 0), stop=(k == len(terms) - 1))
                mm.then_inc(mm_done, 1)

            pe.wait_ge(tower_in, 16 * TOWER_LOADS)
            for p in range(PASSES):
                pe.wait_ge(pij_ready, QUARTERS * (p + 1))
                for m in range(4):
                    layer_bank(P, [(w1d_sb[:, P * m:P * (m + 1)], dense_sb[:, p * ROWS:(p + 1) * ROWS])]
                               + [(w_eff[:, c, P * m:P * (m + 1)], pij_sb[p][:, c, :]) for c in range(QUARTERS)])
            for p in range(PASSES):
                pe.wait_ge(act_done, 4 * p + 4)
                for m in range(2):
                    layer_bank(P, [(w2_sb[:, c, P * m:P * (m + 1)], h1_sb[p][:, c, :]) for c in range(4)])
            for p in range(PASSES):
                pe.wait_ge(act_done, 8 + 2 * p + 2)
                layer_bank(1, [(w3_sb[:, c:c + 1], h2_sb[p][:, c, :]) for c in range(2)])

        @block.vector
        def _(dve):
            def split_k(c):
                dve.wait_ge(k_hi_done, c + 1)
                nc.vector.tensor_tensor(ksplit[c % 2][:, 1, :].bitcast(F32R), ksplit[c % 2][:, 1, :],
                                        ksplit[c % 2][:, 0, :], ALU.subtract).then_inc(k_lo_done, 1)

            def split_x(b):
                dve.wait_ge(x_hi_done, b + 1)
                nc.vector.tensor_tensor(xsplit[b % 2][:, 1, :], xt[:, b * ROWS:(b + 1) * ROWS],
                                        xsplit[b % 2][:, 0, :].bitcast(F32), ALU.subtract).then_inc(x_lo_done, 1)

            def multiply(s):
                first, m0 = s // STEPS * BLOCKS, PASS_UNITS[2 * s % UNITS][1]
                m1 = PASS_UNITS[2 * s % UNITS + 1][1]
                start = (first + m0) * ROWS
                if m0 == m1:
                    x = xt[:, start:start + ROWS].unsqueeze(1).to_broadcast([P, 2, ROWS])
                else:
                    x = xt[:, start:start + 2 * ROWS].rearrange("p (h n) -> p h n", h=2)
                dve.wait_ge(t_ready, s + 1)
                if s >= BUFS:
                    dve.wait_ge(prod_used, s - BUFS + 1)
                nc.vector.tensor_tensor(prod[:, s % BUFS, :, :], t_ps[:, s % BUFS, :, :], x, ALU.mult)\
                  .then_inc(prod_ready, 1)

            for kind, n in startup_order():
                split_x(n) if kind == "x" else split_k(n)
            for s in range(NSTEPS):
                multiply(s)
                if s in CHUNK_AT:
                    split_k(CHUNK_AT[s])
                if s - 1 in BLOCK_AT and BLOCK_AT[s - 1] < BLOCKS:
                    split_x(BLOCK_AT[s - 1])

        @block.scalar
        def _(act):
            def copy(dst, src):
                return nc.scalar.activation(dst, src, ACT.Copy)

            def round_k(c):
                act.wait_ge(kraw_in[c % 2], 16 * (c // 2 + 1))
                copy(ksplit[c % 2][:, 0, :].bitcast(F32R), ksplit[c % 2][:, 1, :]).then_inc(k_hi_done, 1)

            def prepare_x(b):
                act.wait_ge(transposed, b + 1)
                if b == BLOCKS:
                    act.wait_ge(w_eff_mm, 1)
                copy(xsplit[b % 2][:, 0, :], tp[:])
                copy(xt[:, b * ROWS:(b + 1) * ROWS], tp[:]).then_inc(x_hi_done, 1)
                act.wait_ge(x_lo_done, b + 1)
                for f in (1, 0):
                    for half in range(2):
                        last = copy(xr[64 * half:64 * half + 64, b % XSLOTS, f, :, :],
                                    xsplit[b % 2][64 * f:64 * f + 64, :, :].bitcast(F32))
                    last.then_inc(x_ready, 1)

            for kind, n in startup_order():
                prepare_x(n) if kind == "x" else round_k(n)
                if (kind, n) == ("x", 2):
                    act.wait_ge(w_eff_mm, 1)
                    for m in range(QUARTERS):
                        copy(w_eff[:, m, :], banks[m])
                    for m in range(H1 // P):
                        last = nc.scalar.activation(b_eff[:, m:m + 1], banks[4][:, m:m + 1], ACT.Identity,
                                                    bias=b1_sb[:, m:m + 1])
                    last.then_inc(w_eff_done, 1)

            for s in range(NSTEPS):
                if s + 4 in CHUNK_AT:
                    round_k(CHUNK_AT[s + 4])
                if s in BLOCK_AT:
                    prepare_x(BLOCK_AT[s])
                if 2 * (s + 1) % Q_UNITS == 0:
                    q = 2 * s // Q_UNITS
                    act.wait_ge(prod_used, s + 1)
                    copy(pij_sb[q // QUARTERS][:, q % QUARTERS, :], acc[:]).then_inc(pij_ready, 1)

            count = [0]

            def finish(dst, rows, bias):
                n = count[0]
                count[0] += 1
                act.wait_ge(mm_done, n + 1)
                src = banks[n % len(banks)][0:rows, :]
                if bias is None:
                    copy(dst, src).then_inc(act_done, 1)
                else:
                    nc.scalar.activation(dst, src, ACT.Relu, bias=bias).then_inc(act_done, 1)

            act.wait_ge(w_eff_done, 1)
            act.wait_ge(tower_in, 16 * TOWER_LOADS)
            for p in range(PASSES):
                for m in range(4):
                    finish(h1_sb[p][:, m, :], P, b_eff[:, m:m + 1])
            for p in range(PASSES):
                for m in range(2):
                    finish(h2_sb[p][:, m, :], P, b2_sb[:, m:m + 1])
            for p in range(PASSES):
                finish(y_sb[:, p * ROWS:(p + 1) * ROWS], 1, None)


def lay_out(inputs):
    a = {k: np.asarray(v) for k, v in inputs.items()}
    rows, cols = np.triu_indices(FIELDS, k=1)
    number = {(int(i), int(j)): p for p, (i, j) in enumerate(zip(rows, cols))}
    k_in, w_in = a["L0_rec_kernel"], a["L0_rec_W"]
    kraw = np.zeros((CHUNKS, 2, DIM, CHUNK // 2, 2, DIM), k_in.dtype)
    w_pair = np.zeros((C_OUT, PAIR_ROWS), w_in.dtype)
    for w, unit in enumerate(PASS_UNITS):
        c, v = w // CHUNK, w % CHUNK
        for half, pair in enumerate(unit_pairs(unit)):
            if pair is not None:
                kraw[c, v // 8, :, v % 8, half, :] = k_in[:, number[pair], :]
                w_pair[:, pij_row(w, half)] = w_in[:, number[pair]]
    sel = np.zeros((P, 62), np.float32)
    sel[0:64, 30] = 1.0
    sel[64:128, 31] = 1.0

    def columns(x):
        return np.ascontiguousarray(x.reshape(-1, P).T)

    return {
        "dense_t": np.ascontiguousarray(a["dense_ctx"].T), "ids": a["ids"],
        **{f"tbl_{f}": a[f"tbl_{f}"] for f in range(FIELDS)},
        "w_pair": w_pair, "b_pair": columns(a["L0_rec_b"]),
        "w1": a["W_top1"], "b1": columns(a["b_top1"]), "w2": a["W_top2"], "b2": columns(a["b_top2"]),
        "w3": columns(a["W_top3"]), "kraw": kraw.reshape(CHUNKS, P, 1024),
        "ident": np.eye(P, dtype=np.float32), "sel": sel,
    }


def kernel(**inputs):
    import concourse.bacc as bacc
    from concourse.bass_utils import run_bass_kernel_spmd

    arrays = {f"{k}_dram": np.ascontiguousarray(v) for k, v in lay_out(inputs).items()}
    nc = bacc.Bacc("TRN2", target_bir_lowering=False, num_devices=1)
    d = {k[:-5]: nc.dram_tensor(k, v.shape, mybir.dt.from_np(v.dtype), kind="ExternalInput").ap()
         for k, v in arrays.items()}
    out = nc.dram_tensor("y_dram", (1, BATCH), F32, kind="ExternalOutput").ap()
    build(nc, d["dense_t"], d["ids"], [d[f"tbl_{f}"] for f in range(FIELDS)], d["w_pair"], d["b_pair"], d["w1"],
          d["b1"], d["w2"], d["b2"], d["w3"], d["kraw"], d["ident"], d["sel"], out)
    r = run_bass_kernel_spmd(nc, [arrays], core_ids=[0])
    return np.asarray(r.results[0]["y_dram"]).reshape(BATCH, 1)
```

```python
import numpy as np
import concourse.bass as bass
from concourse import mybir
from contextlib import ExitStack

F32 = mybir.dt.float32
F32R = mybir.dt.float32r
I32 = mybir.dt.int32
ALU = mybir.AluOpType
ACT = mybir.ActivationFunctionType

FIELDS, DIM, BATCH, DENSE = 32, 64, 1024, 16
P = 128
ROWS = 512
PASSES = BATCH // ROWS
BT = ROWS // P
BLOCKS = FIELDS // 2
NBLOCKS = PASSES * BLOCKS
UNITS = FIELDS * (FIELDS - 1) // 4
STEPS = UNITS // 2
NSTEPS = PASSES * STEPS
QUADS = STEPS // 2
NQUADS = PASSES * QUADS
CHUNK = 16
CHUNKS = -(-UNITS // CHUNK)
QUAD_UNITS = 4
KSLOTS = 8
BUFS = 3
AHEAD = 2
K_AHEAD = 3
XSLOTS = 6
URGENT = 6
EARLY = 10
Q_UNITS = 64
QUARTERS = -(-UNITS // Q_UNITS)
Q_QUADS = Q_UNITS // QUAD_UNITS
C_OUT, H1, H2 = 256, 512, 256
PAIR_ROWS = QUARTERS * P


def pass_units():
    def unit(m, j):
        return (m, j, (2 * m, 2 * m + 1))

    units, left = [], None
    for n in range(0, BLOCKS, 2):
        if left:
            units += [left, unit(n - 1, 2 * n + 1)]
            left = unit(n - 1, 2 * n)
        for m in range(n - 1 if left else n):
            units += [unit(m, 2 * n + 1), unit(m, 2 * n)]
        if left:
            units += [left, unit(n, 2 * n + 2)]
            left = None
        else:
            left = unit(n, 2 * n + 2)
        second = [unit(m, j) for m in range(n) for j in (2 * n + 3, 2 * n + 2)]
        units += second[:8] + [(None, 2 * n + 1, (2 * n, 2 * n + 3)), (None, 2 * n + 3, (2 * n, 2 * n + 2))]
        units += second[8:]
    return units


PASS_UNITS = pass_units()
assert len(PASS_UNITS) == UNITS


def pij_row(w, half):
    q, v = w // Q_UNITS, w % Q_UNITS
    return P * q + 32 * (v % 4) + 2 * (v // 4) + half


FREE_ROW, FREE_ROWS = 2 * (UNITS % Q_UNITS // 4), DENSE // 4
assert FREE_ROW + FREE_ROWS == 32


def step_units(s):
    w = 2 * (s % STEPS)
    return PASS_UNITS[w:w + 2], s // STEPS * BLOCKS


MIXED_STEP = [s for s in range(NSTEPS) if step_units(s)[0][0][0] is None]


def closes_quarter(k):
    return k % QUADS % Q_QUADS == Q_QUADS - 1 or k % QUADS == QUADS - 1


def block_places():
    first, last = {}, {}
    for s in range(NSTEPS):
        units, start = step_units(s)
        for _, j, factors in units:
            for f in (j,) + factors:
                first.setdefault(start + f // 2, s)
            last[start + j // 2] = s
    places = {AHEAD - 1: -1}
    for b in range(AHEAD, NBLOCKS):
        places[b] = places[b - 1] + 6
        if b < BLOCKS:
            places[b] = min(places[b], max(places[b - 1] + 2, first[b] - b + 2))
        earliest = max(places[b - 1], last.get(b - XSLOTS, -1)) + 1
        places[b] = max(places[b], earliest)
        for k in range(1, NQUADS):
            if closes_quarter(k) and 2 * k - 2 <= places[b] < 2 * k + 4:
                if 2 * k + 4 <= first[b] - 6:
                    places[b] = 2 * k + 4
                elif 2 * k - 3 >= earliest:
                    places[b] = 2 * k - 3
        assert places[b - 1] < places[b] <= first[b]
    return places


BLOCK_PLACES = block_places()
BLOCK_AT = {s: b for b, s in BLOCK_PLACES.items()}
MIXED_AT = {max(s - 10, BLOCK_PLACES[2 * t + 1], MIXED_STEP[t - 1] + 1 if t else -1): t
            for t, s in enumerate(MIXED_STEP)}
assert len(MIXED_AT) == NBLOCKS // 2
STARTUP = [("k", 0), ("k", 1), ("x", 0), ("k", 2), ("x", 1)]
CHUNK_AT = {max(CHUNK // QUAD_UNITS * (c - K_AHEAD) - 3, 0): c for c in range(K_AHEAD, CHUNKS)}
SPLIT_AT = {k + (2 if k > 1 else 0): c for k, c in CHUNK_AT.items()}


def build(nc, dense_t, ids, tables, w_pair, b_pair, w1, b1, w2, b2, w3, kraw, ident_in, sel_in, out):
    k_scratch = nc.dram_tensor("k_split", (CHUNKS, 2, 2, DIM, 1024), F32, kind="Internal").ap()

    ctx = ExitStack()
    with ctx:
        def sb(name, shape, dt=F32):
            return ctx.enter_context(nc.sbuf_tensor(name, shape, dt))

        def sem(name):
            return ctx.enter_context(nc.semaphore(name))

        xt = sb("xt", [P, NBLOCKS * ROWS])
        xr = sb("xr", [P, XSLOTS, 2, 2, ROWS], F32R)
        gathered = [sb(f"gathered{i}", [P, BT, P]) for i in range(2)]
        xsplit = [sb(f"xsplit{i}", [P, 2, ROWS], F32R) for i in range(2)]
        kslot = [sb(f"kslot{i}", [P, QUAD_UNITS, P], F32R) for i in range(KSLOTS)]
        ksplit = [sb(f"ksplit{i}", [P, 2, 1024]) for i in range(2)]
        prod = sb("prod", [P, 4, 2, ROWS])
        pij_sb = [sb(f"pij{p}", [P, QUARTERS, ROWS]) for p in range(PASSES)]
        w_eff = sb("w_eff", [P, QUARTERS, H1])
        b_eff = sb("b_eff", [P, H1 // P])
        b1_sb = sb("b1_sb", [P, H1 // P])
        bp_sb = sb("bp_sb", [P, C_OUT // P])
        ident = sb("ident", [P, P])
        sel = sb("sel", [P, 62])
        mixed = sb("mixed", [P, 2, ROWS])
        idx = sb("idx", [P, BATCH // P, FIELDS], I32)

        def part_of(start, rows, cols):
            return xt[0:rows, start:start + cols], start + cols

        second = BLOCKS * ROWS
        wp_sb, at = part_of(second, P, 2 * PAIR_ROWS)
        w1_sb, at = part_of(at, P, 2 * H1)
        wp_sb = wp_sb.rearrange("p (c n) -> p c n", c=2)
        w1_sb = w1_sb.rearrange("p (c n) -> p c n", c=2)
        assert at <= second + 4 * ROWS
        w2_sb, at = part_of(0, P, 4 * H2)
        w2_sb = w2_sb.rearrange("p (c n) -> p c n", c=4)
        w3_sb, at = part_of(at, P, 2)
        b2_sb, at = part_of(at, P, 2)
        TOWER_LOADS = 3
        h1_sb = [xt[:, second + 4 * p * ROWS:second + 4 * (p + 1) * ROWS].rearrange("p (c n) -> p c n", c=4)
                 for p in range(PASSES)]
        h2_sb = [xt[:, second + (8 + 2 * p) * ROWS:second + (10 + 2 * p) * ROWS].rearrange("p (c n) -> p c n", c=2)
                 for p in range(PASSES)]
        y_sb = ksplit[0][0:1, 0, 0:BATCH]

        t_ps = ctx.enter_context(nc.psum_tensor("t_ps", [P, BUFS, 2, ROWS], F32))
        acc = ctx.enter_context(nc.psum_tensor("acc", [P, ROWS], F32))
        tp = ctx.enter_context(nc.psum_tensor("tp", [P, ROWS], F32))
        banks = [t_ps[:, i // 2, i % 2, :] for i in range(2 * BUFS)]

        consts_in = sem("consts_in")
        idx_in = sem("idx_in")
        w_in = sem("w_in")
        block_in = [sem(f"block_in{i}") for i in range(2)]
        transposed = sem("transposed")
        x_hi_done = sem("x_hi_done")
        x_lo_done = sem("x_lo_done")
        x_odd_ready = sem("x_odd_ready")
        x_even_early = sem("x_even_early")
        x_even_ready = sem("x_even_ready")
        mixed_ready = sem("mixed_ready")
        kraw_in = [sem(f"kraw_in{i}") for i in range(2)]
        k_hi_done = sem("k_hi_done")
        k_lo_done = sem("k_lo_done")
        k_stored = [sem(f"k_stored{i}") for i in range(2)]
        kslot_in = [sem(f"kslot_in{i}") for i in range(KSLOTS)]
        t_ready = sem("t_ready")
        prod_ready = sem("prod_ready")
        summed = sem("summed")
        pij_ready = sem("pij_ready")
        w_eff_mm = sem("w_eff_mm")
        w_eff_done = sem("w_eff_done")
        w_eff_in = sem("w_eff_in")
        dense_in = [sem(f"dense_in{p}") for p in range(PASSES)]
        tower_in = sem("tower_in")
        mm_done = sem("mm_done")
        act_done = sem("act_done")
        out_done = sem("out_done")

        block = ctx.enter_context(nc.Block())

        @block.sync
        def _(sp):
            def load_raw(c):
                sp.dma_start(ksplit[c % 2][:, 1, :], kraw[c, :, :]).then_inc(kraw_in[c % 2], 16)

            def store_split(c):
                sp.wait_ge(k_lo_done, c + 1)
                for a in range(2):
                    sp.dma_start(k_scratch[c, a, :, :, :].rearrange("s d x -> d s x"),
                                 ksplit[c % 2][64 * a:64 * a + 64, :, :]).then_inc(k_stored[c % 2], 16)

            def load_next_raw(c):
                sp.wait_ge(k_stored[c % 2], 32 * (c // 2 + 1))
                if c + 2 < CHUNKS:
                    load_raw(c + 2)

            def load_slot(k):
                c, v = divmod(k % QUADS * QUAD_UNITS, CHUNK)
                src = k_scratch[c, v // 8, :, :, P * (v % 8):P * (v % 8 + QUAD_UNITS)]
                sp.dma_start(kslot[k % KSLOTS][:].rearrange("p u n -> p (u n)").bitcast(F32),
                             src.rearrange("s d x -> (s d) x")).then_inc(kslot_in[k % KSLOTS], 16)

            def free_rows(x, g):
                return x[32 * g + FREE_ROW:32 * g + 32, QUARTERS - 1, :]

            def load_dense(p):
                sp.wait_ge(pij_ready, QUARTERS * (p + 1))
                for g in range(4):
                    sp.dma_start(free_rows(pij_sb[p], g), dense_t[FREE_ROWS * g:FREE_ROWS * (g + 1),
                                                                  p * ROWS:(p + 1) * ROWS]).then_inc(dense_in[p], 16)

            sp.dma_start(idx[:], ids.rearrange("(t p) f -> p t f", p=P)).then_inc(idx_in, 16)
            load_raw(0)
            load_raw(1)
            sp.dma_start(ident[:], ident_in).then_inc(consts_in, 16)
            sp.dma_start(sel[:], sel_in).then_inc(consts_in, 16)
            for dst, src in ((wp_sb, w_pair.rearrange("(c p) n -> p c n", p=P)),
                             (w1_sb, w1[0:C_OUT, :].rearrange("(c p) n -> p c n", p=P)),
                             (bp_sb[:], b_pair), (b1_sb[:], b1)):
                sp.dma_start(dst, src).then_inc(w_in, 16)
            for c in range(K_AHEAD):
                store_split(c)
                load_next_raw(c)
                if c < 2:
                    for k in range(CHUNK // QUAD_UNITS * c, CHUNK // QUAD_UNITS * (c + 1)):
                        load_slot(k)

            for k in range(NQUADS):
                if k - 1 in SPLIT_AT:
                    store_split(SPLIT_AT[k - 1])
                if k - 2 in SPLIT_AT:
                    load_next_raw(SPLIT_AT[k - 2])
                if k + KSLOTS < NQUADS:
                    sp.wait_ge(t_ready, 2 * k + 2)
                    load_slot(k + KSLOTS)
                if k == 2 * Q_QUADS:
                    sp.wait_ge(w_eff_done, 1)
                    for g in range(4):
                        row = C_OUT + FREE_ROWS * g
                        sp.dma_start(free_rows(w_eff, g), w1[row:row + FREE_ROWS, :]).then_inc(w_eff_in, 16)
                if k == QUADS + 6:
                    load_dense(0)
                if k == QUADS + 4:
                    sp.wait_ge(prod_ready, STEPS)
                    for dst, src in ((w2_sb, w2.rearrange("(c p) n -> p c n", p=P)), (w3_sb, w3), (b2_sb, b2)):
                        sp.dma_start(dst, src).then_inc(tower_in, 16)

            load_dense(PASSES - 1)
            sp.wait_ge(act_done, PASSES * (4 + 2 + 1))
            sp.dma_start(out, y_sb).then_inc(out_done, 16)
            sp.wait_ge(out_done, 16)

        @block.gpsimd
        def _(pool):
            pool.wait_ge(idx_in, 16)
            for b in range(NBLOCKS):
                p, n = b // BLOCKS, b % BLOCKS
                if b >= 2:
                    pool.wait_ge(transposed, b - 1)
                for t in range(BT):
                    for half in range(2):
                        f = 2 * n + half
                        pool.indirect_dma_start(
                            out=gathered[b % 2][:, t, DIM * half:DIM * (half + 1)], out_offset=None,
                            in_=tables[f],
                            in_offset=bass.IndirectOffsetOnAxis(ap=idx[:, p * BT + t, f:f + 1], axis=0),
                        ).then_inc(block_in[b % 2], 16)

        @block.tensor
        def _(pe):
            def transpose_block(b):
                pe.wait_ge(block_in[b % 2], P * (b // 2 + 1))
                if b:
                    pe.wait_ge(x_hi_done, b)
                for t in range(BT):
                    mm = pe.transpose(tp[:, t * P:(t + 1) * P], gathered[b % 2][:, t, :], ident[:])
                mm.then_inc(transposed, 1)

            def fold_weights(quarters):
                for m in quarters:
                    for c in range(2):
                        pe.matmul(banks[m], wp_sb[:, c, P * m:P * (m + 1)], w1_sb[:, c, :],
                                  start=(c == 0), stop=(c == 1))

            def fold_bias():
                for m in range(H1 // P):
                    for c in range(2):
                        mm = pe.matmul(banks[4][:, m:m + 1], w1_sb[:, c, P * m:P * (m + 1)], bp_sb[:, c:c + 1],
                                       start=(c == 0), stop=(c == 1))
                mm.then_inc(w_eff_mm, 1)

            seen = {}

            def wait_for_x(b, odd):
                if b <= seen.get(odd, -1):
                    return
                seen[odd] = b
                if odd:
                    pe.wait_ge(x_odd_ready, b + 1)
                elif b < EARLY:
                    pe.wait_ge(x_even_early, b + 1)
                else:
                    pe.wait_ge(x_even_ready, b - EARLY + 1)

            def products(s):
                k = s // 2
                if s % 2 == 0:
                    pe.wait_ge(kslot_in[k % KSLOTS], 16 * (k // KSLOTS + 1))
                if s >= BUFS and (s % 2 or s < 2 * BUFS):
                    pe.wait_ge(prod_ready, s - BUFS + 1)
                units, start = step_units(s)
                for h, (_, j, _) in enumerate(units):
                    wait_for_x(start + j // 2, j % 2)
                    for part in range(2):
                        mm = pe.matmul(t_ps[:, s % BUFS, h, :], kslot[k % KSLOTS][:, 2 * (s % 2) + h, :],
                                       xr[:, (start + j // 2) % XSLOTS, j % 2, part, :],
                                       start=(part == 0), stop=(part == 1))
                mm.then_inc(t_ready, 1)

            def sum_over_e(k):
                q, c = k % QUADS // Q_QUADS, k % QUADS % Q_QUADS
                if k and c == 0:
                    pe.wait_ge(pij_ready, k // QUADS * QUARTERS + q)
                pe.wait_ge(prod_ready, 2 * k + 2)
                for g in range(QUAD_UNITS):
                    mm = pe.matmul(acc[32 * g:32 * g + 32, :], sel[:, 30 - 2 * c:62 - 2 * c],
                                   prod[:, 2 * (k % 2) + g // 2, g % 2, :],
                                   start=(c == 0), stop=closes_quarter(k))
                mm.then_inc(summed, 1)

            pe.wait_ge(consts_in, 32)
            pe.wait_ge(w_in, 64)
            fold_weights(range(0, 3))
            transpose_block(0)
            fold_weights(range(3, QUARTERS))
            fold_bias()
            transpose_block(1)
            pe.wait_ge(w_eff_done, 1)
            for k in range(NQUADS):
                for s in (2 * k, 2 * k + 1):
                    if s in BLOCK_AT:
                        transpose_block(BLOCK_AT[s])
                    products(s)
                if k:
                    sum_over_e(k - 1)

            count = [0]

            def layer_bank(terms):
                n = count[0]
                count[0] += 1
                if n >= len(banks):
                    pe.wait_ge(act_done, n - len(banks) + 1)
                for k, (w, x) in enumerate(terms):
                    mm = pe.matmul(banks[n % len(banks)], w, x, start=(k == 0), stop=(k == len(terms) - 1))
                mm.then_inc(mm_done, 1)

            def first_layer(p, m):
                layer_bank([(w_eff[:, c, P * m:P * (m + 1)], pij_sb[p][:, c, :]) for c in range(QUARTERS)])

            pe.wait_ge(tower_in, 16 * TOWER_LOADS)
            pe.wait_ge(w_eff_in, 16 * 4)
            pe.wait_ge(dense_in[0], 16 * 4)
            pe.wait_ge(prod_ready, NSTEPS - 1)
            assert (NSTEPS - 2) % BUFS == 0
            first_layer(0, 0)
            sum_over_e(NQUADS - 1)
            for m in range(1, 4):
                first_layer(0, m)
            pe.wait_ge(dense_in[1], 16 * 4)
            for m in range(4):
                first_layer(1, m)
            for p in range(PASSES):
                pe.wait_ge(act_done, 4 * p + 4)
                for m in range(2):
                    layer_bank([(w2_sb[:, c, P * m:P * (m + 1)], h1_sb[p][:, c, :]) for c in range(4)])
            for c in range(2):
                pe.wait_ge(act_done, PASSES * (4 + 2) - 1 + c)
                for p in range(PASSES):
                    mm = pe.matmul(banks[p][32 * p:32 * p + 1, :], w3_sb[:, c:c + 1], h2_sb[p][:, c, :],
                                   start=(c == 0), stop=(c == 1))
            mm.then_inc(mm_done, 1)

        @block.vector
        def _(dve):
            def split_k(c):
                dve.wait_ge(k_hi_done, c + 1)
                nc.vector.tensor_tensor(ksplit[c % 2][:, 1, :].bitcast(F32R), ksplit[c % 2][:, 1, :],
                                        ksplit[c % 2][:, 0, :], ALU.subtract).then_inc(k_lo_done, 1)

            def split_x(b):
                dve.wait_ge(x_hi_done, b + 1)
                nc.vector.tensor_tensor(xsplit[b % 2][:, 1, :], xt[:, b * ROWS:(b + 1) * ROWS],
                                        xsplit[b % 2][:, 0, :].bitcast(F32), ALU.subtract).then_inc(x_lo_done, 1)
                if b < EARLY:
                    dve.wait_ge(x_lo_done, b + 1)
                    for half in range(2):
                        last = nc.vector.tensor_copy(xr[64 * half:64 * half + 64, b % XSLOTS, 0, :, :],
                                                     xsplit[b % 2][0:64, :, :].bitcast(F32))
                    last.then_inc(x_even_early, 1)

            def multiply(s):
                ((m0, _, _), (m1, _, _)), first = step_units(s)
                if m0 is None:
                    dve.wait_ge(mixed_ready, MIXED_STEP.index(s) + 1)
                    x = mixed[:]
                elif m0 == m1:
                    start = (first + m0) * ROWS
                    x = xt[:, start:start + ROWS].unsqueeze(1).to_broadcast([P, 2, ROWS])
                else:
                    x = xt[:, (first + m0) * ROWS:(first + 2 * m1 - m0) * ROWS]
                    x = x.rearrange("p (h n) -> p h n", h=2)[:, :, 0:ROWS]
                dve.wait_ge(t_ready, s + 1)
                if s % 2 == 0 and s >= 4:
                    dve.wait_ge(summed, s // 2 - 1)
                nc.vector.tensor_tensor(prod[:, s % 4, :, :], t_ps[:, s % BUFS, :, :], x, ALU.mult)\
                  .then_inc(prod_ready, 1)

            for kind, n in STARTUP:
                split_x(n) if kind == "x" else split_k(n)
            for k in range(NQUADS):
                for s in (2 * k, 2 * k + 1):
                    if BLOCK_AT.get(s, NBLOCKS) < URGENT:
                        split_x(BLOCK_AT[s])
                    multiply(s)
                    if BLOCK_AT.get(s - 1, -1) >= URGENT:
                        split_x(BLOCK_AT[s - 1])
                if k in SPLIT_AT:
                    split_k(SPLIT_AT[k])

        @block.scalar
        def _(act):
            def copy(dst, src):
                return nc.scalar.activation(dst, src, ACT.Copy)

            def round_k(c):
                act.wait_ge(kraw_in[c % 2], 16 * (c // 2 + 1))
                copy(ksplit[c % 2][:, 0, :].bitcast(F32R), ksplit[c % 2][:, 1, :]).then_inc(k_hi_done, 1)

            def prepare_x(b):
                act.wait_ge(transposed, b + 1)
                if b == BLOCKS:
                    act.wait_ge(w_eff_mm, 1)
                if b - 2 in range(EARLY):
                    act.wait_ge(x_even_early, b - 1)
                copy(xsplit[b % 2][:, 0, :], tp[:])
                copy(xt[:, b * ROWS:(b + 1) * ROWS], tp[:]).then_inc(x_hi_done, 1)
                act.wait_ge(x_lo_done, b + 1)
                for f in (1, 0) if b >= EARLY else (1,):
                    for half in range(2):
                        last = copy(xr[64 * half:64 * half + 64, b % XSLOTS, f, :, :],
                                    xsplit[b % 2][64 * f:64 * f + 64, :, :].bitcast(F32))
                    last.then_inc(x_odd_ready if f else x_even_ready, 1)

            def mix(t):
                if t:
                    act.wait_ge(prod_ready, MIXED_STEP[t - 1] + 1)
                first, second = (xt[:, b * ROWS:(b + 1) * ROWS] for b in (2 * t, 2 * t + 1))
                copy(mixed[0:DIM, :, :], first[0:DIM, :].unsqueeze(1).to_broadcast([DIM, 2, ROWS]))
                copy(mixed[DIM:P, 0, :], second[DIM:P, :])
                copy(mixed[DIM:P, 1, :], second[0:DIM, :]).then_inc(mixed_ready, 1)

            for kind, n in STARTUP:
                prepare_x(n) if kind == "x" else round_k(n)
                if (kind, n) == ("x", 0):
                    act.wait_ge(w_eff_mm, 1)
                    for m in range(QUARTERS):
                        copy(w_eff[:, m, :], banks[m])
                    for m in range(H1 // P):
                        last = nc.scalar.activation(b_eff[:, m:m + 1], banks[4][:, m:m + 1], ACT.Identity,
                                                    bias=b1_sb[:, m:m + 1])
                    last.then_inc(w_eff_done, 1)

            mix(0)
            for k in range(NQUADS):
                for s in (2 * k, 2 * k + 1):
                    if s in BLOCK_AT:
                        prepare_x(BLOCK_AT[s])
                    if s in MIXED_AT:
                        mix(MIXED_AT[s])
                if k in CHUNK_AT:
                    round_k(CHUNK_AT[k])
                if closes_quarter(k):
                    act.wait_ge(summed, k + 1)
                    copy(pij_sb[k // QUADS][:, k % QUADS // Q_QUADS, :], acc[:]).then_inc(pij_ready, 1)

            count = [0]

            def finish(dst, bias):
                n = count[0]
                count[0] += 1
                act.wait_ge(mm_done, n + 1)
                nc.scalar.activation(dst, banks[n % len(banks)], ACT.Relu, bias=bias).then_inc(act_done, 1)

            act.wait_ge(w_eff_done, 1)
            act.wait_ge(tower_in, 16 * TOWER_LOADS)
            for p in range(PASSES):
                for m in range(4):
                    finish(h1_sb[p][:, m, :], b_eff[:, m:m + 1])
            for p in range(PASSES):
                for m in range(2):
                    finish(h2_sb[p][:, m, :], b2_sb[:, m:m + 1])
            act.wait_ge(mm_done, PASSES * (4 + 2) + 1)
            for p in range(PASSES):
                copy(y_sb[:, p * ROWS:(p + 1) * ROWS], banks[p][32 * p:32 * p + 1, :]).then_inc(act_done, 1)


def lay_out(inputs):
    a = {k: np.asarray(v) for k, v in inputs.items()}
    rows, cols = np.triu_indices(FIELDS, k=1)
    number = {(int(i), int(j)): p for p, (i, j) in enumerate(zip(rows, cols))}
    k_in, w_in = a["L0_rec_kernel"], a["L0_rec_W"]
    kraw = np.zeros((CHUNKS, 2, DIM, CHUNK // 2, 2, DIM), k_in.dtype)
    w_pair = np.zeros((C_OUT, PAIR_ROWS), w_in.dtype)
    for w, (_, j, factors) in enumerate(PASS_UNITS):
        c, v = w // CHUNK, w % CHUNK
        for half, i in enumerate(factors):
            n = number[min(i, j), max(i, j)]
            k_pair = k_in[:, n, :]
            kraw[c, v // 8, :, v % 8, half, :] = k_pair if i < j else k_pair.T
            w_pair[:, pij_row(w, half)] = w_in[:, n]
    sel = np.zeros((P, 62), np.float32)
    sel[0:64, 30] = 1.0
    sel[64:128, 31] = 1.0

    def columns(x):
        return np.ascontiguousarray(x.reshape(-1, P).T)

    return {
        "dense_t": np.ascontiguousarray(a["dense_ctx"].T), "ids": a["ids"],
        **{f"tbl_{f}": a[f"tbl_{f}"] for f in range(FIELDS)},
        "w_pair": w_pair, "b_pair": columns(a["L0_rec_b"]),
        "w1": a["W_top1"], "b1": columns(a["b_top1"]), "w2": a["W_top2"], "b2": columns(a["b_top2"]),
        "w3": columns(a["W_top3"]), "kraw": kraw.reshape(CHUNKS, P, 1024),
        "ident": np.eye(P, dtype=np.float32), "sel": sel,
    }


def kernel(**inputs):
    import concourse.bacc as bacc
    from concourse.bass_utils import run_bass_kernel_spmd

    arrays = {f"{k}_dram": np.ascontiguousarray(v) for k, v in lay_out(inputs).items()}
    nc = bacc.Bacc("TRN2", target_bir_lowering=False, num_devices=1)
    d = {k[:-5]: nc.dram_tensor(k, v.shape, mybir.dt.from_np(v.dtype), kind="ExternalInput").ap()
         for k, v in arrays.items()}
    out = nc.dram_tensor("y_dram", (1, BATCH), F32, kind="ExternalOutput").ap()
    build(nc, d["dense_t"], d["ids"], [d[f"tbl_{f}"] for f in range(FIELDS)], d["w_pair"], d["b_pair"], d["w1"],
          d["b1"], d["w2"], d["b2"], d["w3"], d["kraw"], d["ident"], d["sel"], out)
    r = run_bass_kernel_spmd(nc, [arrays], core_ids=[0])
    return np.asarray(r.results[0]["y_dram"]).reshape(BATCH, 1)
```
